# Optimizing a Trainium2 kernel written in Bass

```python
import numpy as np
import jax
import jax.numpy as jnp

def _softmax(x, axis=-1):
    return jax.nn.softmax(x, axis=axis)

def _gelu(x):
    return jax.nn.gelu(x, approximate=True)

def _silu(x):
    return jax.nn.silu(x)

def _sigmoid(x):
    return jax.nn.sigmoid(x)

def _layernorm(x, axis=-1, eps=1e-05):
    m = jnp.mean(x, axis=axis, keepdims=True)
    v = jnp.var(x, axis=axis, keepdims=True)
    return (x - m) / jnp.sqrt(v + eps)

def _scatter_add(tgt, idx, src, axis=0):
    return tgt.at[idx].add(src)

def _segment_sum(src, seg, n):
    return jax.ops.segment_sum(src, seg, n)
kernel_name = 'mk_adaln_ffn_d1_seqx_r8_09266a'

def setup_inputs(seed: int=0):
    np.random.seed(seed)
    _w = jnp.asarray

    def _rec_inputs():
        import jax
        import jax.numpy as jnp
        _rk = jax.random.key(seed)
        x = -7.109e-05 + 0.9999 * jax.random.normal(jax.random.fold_in(_rk, 1), (32, 32, 512), jnp.float32)
        _lenS = 32 - jax.random.randint(jax.random.fold_in(_rk, 7), (32,), 0, max(1, 32 // 4) + 1, jnp.int32)
        _lenS2 = 32 - jax.random.randint(jax.random.fold_in(_rk, 8), (32,), 0, max(1, 32 // 4) + 1, jnp.int32)
        itok_B_0_15 = jax.random.randint(jax.random.fold_in(_rk, 11), (32,), 0, 16, jnp.int32)
        return (x, itok_B_0_15)
    x, itok_B_0_15 = _rec_inputs()

    def _L0_cond_setup():
        import jax, jax.numpy as jnp
        import numpy as np
        B, C, T = (64, 32, 512)
        S, D = (16, 32)
        key = jax.random.key(seed)
        k1, k2, k3 = jax.random.split(key, 3)
        x = jax.random.normal(k1, (B, C, T), dtype=jnp.float32)
        condition = jax.random.randint(k2, (B,), 0, S, dtype=jnp.int64)
        bound = float(np.sqrt(6.0 / C))
        weights = jax.random.uniform(k3, (S, C, D), dtype=jnp.float32, minval=-bound, maxval=bound)
        return {'x': x, 'condition': condition, 'weights': weights}
    _L0_cond_all = _L0_cond_setup()
    _L0_cond_in = {k: v for k, v in _L0_cond_all.items() if k in ('weights',)}
    del _L0_cond_all

    def _L0_ffn_setup():
        import jax, jax.numpy as jnp
        import numpy as np
        HID, INTER = (512, 1792)
        B, S = (2, 256)

        def _binary_diff_weight(w, base):
            d = w - base
            coeff = jnp.mean(jnp.abs(d))
            return base + coeff * jnp.sign(d)
        key = jax.random.key(seed)
        ks = jax.random.split(key, 7)
        return {'hidden_states': jax.random.normal(ks[0], (B, S, HID), dtype=jnp.float32), 'w1': jax.random.normal(ks[1], (INTER, HID), dtype=jnp.float32) * 0.02, 'mean_w1': jax.random.normal(ks[2], (INTER, HID), dtype=jnp.float32) * 0.02, 'w2': jax.random.normal(ks[3], (HID, INTER), dtype=jnp.float32) * 0.02, 'mean_w2': jax.random.normal(ks[4], (HID, INTER), dtype=jnp.float32) * 0.02, 'w3': jax.random.normal(ks[5], (INTER, HID), dtype=jnp.float32) * 0.02, 'mean_w3': jax.random.normal(ks[6], (INTER, HID), dtype=jnp.float32) * 0.02}
    _L0_ffn_all = _L0_ffn_setup()
    _L0_ffn_in = {k: v for k, v in _L0_ffn_all.items() if k in ('w1', 'mean_w1', 'w2', 'mean_w2', 'w3', 'mean_w3')}
    del _L0_ffn_all
    return {'x': x, 'itok_B_0_15': itok_B_0_15, 'L0_cond_weights': _L0_cond_in['weights'], 'L0_ffn_w1': _L0_ffn_in['w1'], 'L0_ffn_mean_w1': _L0_ffn_in['mean_w1'], 'L0_ffn_w2': _L0_ffn_in['w2'], 'L0_ffn_mean_w2': _L0_ffn_in['mean_w2'], 'L0_ffn_w3': _L0_ffn_in['w3'], 'L0_ffn_mean_w3': _L0_ffn_in['mean_w3']}

def reference(x, itok_B_0_15, L0_cond_weights, L0_ffn_w1, L0_ffn_mean_w1, L0_ffn_w2, L0_ffn_mean_w2, L0_ffn_w3, L0_ffn_mean_w3):
    import jax
    import jax.numpy as jnp

    def _L0_cond_ref(x, condition, weights):
        import jax, jax.numpy as jnp
        import numpy as np
        B, C, T = (64, 32, 512)
        S, D = (16, 32)
        W = weights[condition]
        return jnp.einsum('bct,bcd->bdt', x, W)

    def _L0_ffn_ref(hidden_states, w1, mean_w1, w2, mean_w2, w3, mean_w3):
        import jax, jax.numpy as jnp
        import numpy as np
        HID, INTER = (512, 1792)
        B, S = (2, 256)

        def _binary_diff_weight(w, base):
            d = w - base
            coeff = jnp.mean(jnp.abs(d))
            return base + coeff * jnp.sign(d)
        W1 = _binary_diff_weight(w1, mean_w1)
        W2 = _binary_diff_weight(w2, mean_w2)
        W3 = _binary_diff_weight(w3, mean_w3)
        gate = jnp.einsum('bsh,ih->bsi', hidden_states, W1)
        up = jnp.einsum('bsh,ih->bsi', hidden_states, W3)
        h = jax.nn.silu(gate) * up
        return jnp.einsum('bsi,hi->bsh', h, W2)
    x = x + _L0_ffn_ref(_L0_cond_ref(x, itok_B_0_15, L0_cond_weights), L0_ffn_w1, L0_ffn_mean_w1, L0_ffn_w2, L0_ffn_mean_w2, L0_ffn_w3, L0_ffn_mean_w3)
    return x

_drawn_inputs = setup_inputs


def setup_inputs(seed=0):
    import zlib

    import numpy as np

    out = dict(_drawn_inputs(seed))
    spreads = {}
    factors = {}
    for name, (base, spread) in spreads.items():
        noise = np.random.default_rng([zlib.crc32(name.encode()), seed]).standard_normal(out[name].shape)
        drawn = base * np.exp(spread * noise) if base else spread * noise
        out[name] = jnp.asarray(drawn.astype(out[name].dtype))
    for name, factor in factors.items():
        out[name] = (out[name] * factor).astype(out[name].dtype)
    return out
```

```python
from contextlib import ExitStack

import concourse.bass as bass
from concourse import mybir

P = 128
F32 = mybir.dt.float32
F32R = mybir.dt.float32r
BF16 = mybir.dt.bfloat16
I32 = mybir.dt.int32
ALU = mybir.AluOpType
ACT = mybir.ActivationFunctionType
AX_X = mybir.AxisListType.X


def adaln_ffn(nc, x, cond, cond_w, w1, m1, w3, m3, w2, m2, out):
    HIDDEN = x.shape[2]
    TOKENS = x.shape[0] * x.shape[1]
    C = x.shape[1]
    TILES = w1.shape[1]
    UNIT = w1.shape[2]
    KT = HIDDEN // P
    GROUPS = TOKENS // P
    CANDIDATES = cond_w.shape[1]
    PER_GROUP = P // C
    HALF = TOKENS // 2
    HG = GROUPS // 2
    COUNT = TILES * UNIT * P
    CHUNK = 2 * UNIT
    CHUNKS = TILES // 2
    PAIRS = TILES // 2 - 1
    assert UNIT == HIDDEN == HALF == 512 and TILES % 2 == 0 and PER_GROUP * C == P

    with ExitStack() as ctx:
        def sb(name, shape, dt):
            return ctx.enter_context(nc.sbuf_tensor(name, shape, dt))

        def sem(name):
            return ctx.enter_context(nc.semaphore(name))

        y_high = sb("y_high", [P, KT, TOKENS], F32R)
        y_low = sb("y_low", [P, KT, TOKENS], F32R)
        hidden = sb("hidden", [P, TILES * TOKENS], F32)
        base = [sb(f"base{i}", [P, TILES * UNIT], F32) for i in range(2)]
        sign = [sb(f"sign{i}", [P, TILES * UNIT], BF16) for i in range(2)]
        stage = sb("stage", [P, 2, UNIT], F32)
        w_high = sb("w_high", [P, 2, UNIT], F32R)
        w_low = sb("w_low", [P, 2, UNIT], F32R)
        h_high = sb("h_high", [P, 2, HALF], F32R)
        h_low = sb("h_low", [P, 2, HALF], F32R)
        mean_of = sb("mean_of", [P, P], F32)
        abs_sum = sb("abs_sum", [P, 3, TILES], F32)
        coeff = sb("coeff", [P, 3], F32)
        itok = sb("itok", [P, GROUPS], I32)

        w1_diff = hidden[:, 0:TILES * UNIT]
        at = TILES * UNIT
        x_in = hidden[:, at:at + GROUPS * HIDDEN].rearrange("p (g t) -> p g t", g=GROUPS)
        at += GROUPS * HIDDEN
        mix = hidden[:, at:at + GROUPS * C].rearrange("p (g d) -> p g d", g=GROUPS)
        at += GROUPS * C
        mix_diag = hidden[:, at:at + GROUPS * P].rearrange("p (g n) -> p g n", g=GROUPS)
        at += GROUPS * P
        choices = hidden[:, at:at + CANDIDATES * C].rearrange("p (s d) -> p s d", s=CANDIDATES)
        at += CANDIDATES * C
        assert at <= TILES * TOKENS
        number = stage[:, 0, 0:CANDIDATES * GROUPS].bitcast(I32).rearrange("p (s g) -> p s g", g=GROUPS)
        chosen = stage[:, 1, 0:CANDIDATES * GROUPS].bitcast(I32).rearrange("p (s g) -> p s g", g=GROUPS)
        result = base[1][:, 0:GROUPS * HIDDEN].rearrange("p (g t) -> p g t", g=GROUPS)

        bank = [ctx.enter_context(nc.psum_tensor(f"bank{i}", [P, 512], F32)) for i in range(8)]
        Y_BANKS = [4, 5, 6]
        MEAN_BANK = 7

        itok_in = sem("itok_in")
        choices_in = sem("choices_in")
        number_ready = sem("number_ready")
        diag_zeroed = sem("diag_zeroed")
        x_loaded = [sem(f"x_loaded{i}") for i in range(2)]
        w1_in = [sem(f"w1_in{c}") for c in range(CHUNKS)]
        stream_in = [sem(f"stream_in{i}") for i in range(2)]
        residual_in = sem("residual_in")
        out_done = sem("out_done")
        chosen_ready = sem("chosen_ready")
        mix_chosen = sem("mix_chosen")
        mix_ready = sem("mix_ready")
        const_ready = sem("const_ready")
        y_high_ready = sem("y_high_ready")
        diff_ready = sem("diff_ready")
        sign_done = sem("sign_done")
        abs_done = sem("abs_done")
        mean_summed = sem("mean_summed")
        coeff_ready = sem("coeff_ready")
        full_ready = sem("full_ready")
        high_ready = sem("high_ready")
        low_ready = sem("low_ready")
        sums_done = sem("sums_done")
        drained = sem("drained")
        h_high_ready = sem("h_high_ready")
        h_low_ready = sem("h_low_ready")
        group_done = sem("group_done")
        result_ready = sem("result_ready")

        gate, up, down = 0, 1, 2
        mat = {gate: 0, up: 1, down: 0}

        def tile_of(buf, u):
            return buf[:, bass.ds(u * UNIT, UNIT)]

        def hidden_of(u, half):
            return hidden[:, bass.ds(u * TOKENS + half * HALF, HALF)]

        block = ctx.enter_context(nc.Block())

        @block.sync
        def _(sp):
            x_dram = x.rearrange("(g b) c t -> (b c) g t", g=GROUPS)
            for i in range(2):
                g = slice(i * HG, (i + 1) * HG)
                sp.dma_start(x_in[:, g, :], x_dram[:, g, :]).then_inc(x_loaded[i], 16)
            w1_flat = w1.rearrange("p u n -> p (u n)")
            m1_flat = m1.rearrange("p u n -> p (u n)")
            for c in range(CHUNKS):
                s = slice(c * CHUNK, (c + 1) * CHUNK)
                sp.dma_start(w1_diff[:, s], w1_flat[:, s]).then_inc(w1_in[c], 16)
                sp.dma_start(base[0][:, s], m1_flat[:, s]).then_inc(w1_in[c], 16)

            def stream(phase, w, m):
                with sp.Fori(0, TILES // 2) as j:
                    for s in range(2):
                        u = j * 2 + s
                        v = phase * TILES + u
                        sp.wait_ge(sign_done, CHUNKS + v - 1)
                        sp.wait_ge(abs_done, CHUNKS + v - 1)
                        sp.dma_start(stage[:, s, :], w[:, bass.ds(u, 1), :]).then_inc(stream_in[s], 16)
                        sp.dma_start(tile_of(base[mat[phase + 1]], u), m[:, bass.ds(u, 1), :])\
                          .then_inc(stream_in[s], 16)

            stream(gate, w3, m3)
            sp.wait_ge(low_ready, TILES)
            stream(up, w2, m2)
            sp.wait_ge(low_ready, 2 * TILES)
            sp.dma_start(result, x_dram).then_inc(residual_in, 16)
            out_dram = out.rearrange("(g b) c t -> (b c) g t", g=GROUPS)
            for g in range(GROUPS):
                sp.wait_ge(result_ready, g + 1)
                sp.dma_start(out_dram[:, g, :], result[:, g, :]).then_inc(out_done, 16)
            sp.wait_ge(out_done, 16 * GROUPS)

        @block.gpsimd
        def _(pool):
            for b in range(PER_GROUP):
                pool.dma_start(itok[b * C:(b + 1) * C, :], cond[b:b + 1, :].to_broadcast([C, GROUPS]))\
                    .then_inc(itok_in, 16)
            nc.gpsimd.iota(number[:], pattern=[[1, CANDIDATES], [0, GROUPS]], base=0,
                           channel_multiplier=0).then_inc(number_ready, 1)
            nc.gpsimd.memset(mix_diag, 0.0).then_inc(diag_zeroed, 1)

        @block.tensor
        def _(pe):
            pe.wait_ge(mix_ready, PER_GROUP)
            for g in range(GROUPS):
                pe.wait_ge(x_loaded[g // HG], 16)
                if g >= len(Y_BANKS):
                    pe.wait_ge(drained, g - len(Y_BANKS) + 1)
                for k in range(KT):
                    last = nc.tensor.matmul(bank[Y_BANKS[g % len(Y_BANKS)]][:, k * P:(k + 1) * P],
                                            x_in[:, g, k * P:(k + 1) * P], mix_diag[:, g, :],
                                            start=True, stop=True)
                last.then_inc(sums_done, 1)

            def mean(phase, parts):
                pe.wait_ge(abs_done, CHUNKS + phase * TILES)
                nc.tensor.matmul(bank[MEAN_BANK][:, 0:parts], mean_of[:], abs_sum[:, phase, 0:parts],
                                 start=True, stop=True).then_inc(mean_summed, 1)

            def project(phase, u, s):
                step = u + phase * TILES
                pe.wait_ge(low_ready, step + 1)
                for half in range(2):
                    pe.wait_ge(drained, 2 * step + GROUPS - 3 + half)
                    dst = bank[2 * s + half][:]
                    t = slice(half * HALF, (half + 1) * HALF)
                    for k in range(KT):
                        n = slice(k * P, (k + 1) * P)
                        nc.tensor.matmul(dst, w_high[:, s, n], y_high[:, k, t], start=(k == 0), stop=False)
                        nc.tensor.matmul(dst, w_high[:, s, n], y_low[:, k, t], start=False, stop=False)
                        last = nc.tensor.matmul(dst, w_low[:, s, n], y_high[:, k, t], start=False,
                                                stop=(k == KT - 1))
                    last.then_inc(sums_done, 1)

            def contract(u, s, first=False, final=False):
                pe.wait_ge(low_ready, u + 2 * TILES + 1)
                for half in range(2):
                    pe.wait_ge(h_low_ready, u * 2 + half + 1)
                    if first and half == 1:
                        pe.wait_ge(drained, GROUPS + 4 * TILES)
                    for i in range(HG):
                        g = half * HG + i
                        dst = bank[(g + 4) % 8][:]
                        n = slice(i * P, (i + 1) * P)
                        nc.tensor.matmul(dst, h_high[:, half, n], w_high[:, s, :], start=first, stop=False)
                        nc.tensor.matmul(dst, h_high[:, half, n], w_low[:, s, :], start=False, stop=False)
                        last = nc.tensor.matmul(dst, h_low[:, half, n], w_high[:, s, :], start=False,
                                                stop=final)
                        if final:
                            last.then_inc(group_done, 1)
                    if not final:
                        last.then_inc(sums_done, 1)

            pe.wait_ge(const_ready, 1)
            mean(gate, CHUNKS)
            for phase in (gate, up):
                with pe.Fori(0, PAIRS) as j:
                    for s in range(2):
                        project(phase, j * 2 + s, s)
                project(phase, TILES - 2, 0)
                mean(phase + 1, TILES)
                project(phase, TILES - 1, 1)
            contract(0, 0, first=True)
            contract(1, 1)
            with pe.Fori(1, PAIRS) as j:
                for s in range(2):
                    contract(j * 2 + s, s)
            contract(TILES - 2, 0)
            contract(TILES - 1, 1, final=True)

        @block.scalar
        def _(act):
            def y_group(g):
                act.wait_ge(sums_done, g + 1)
                src = bank[Y_BANKS[g % len(Y_BANKS)]][:].rearrange("p (k n) -> p k n", k=KT)
                nc.scalar.copy(y_high[:, :, g * P:(g + 1) * P], src).then_inc(y_high_ready, 1)

            def sign_w1(c):
                s = slice(c * CHUNK, (c + 1) * CHUNK)
                act.wait_ge(diff_ready, c + 1)
                nc.scalar.activation(sign[0][:, s], w1_diff[:, s], ACT.Sign).then_inc(sign_done, 1)

            def signs(phase, u, s):
                act.wait_ge(diff_ready, u + (CHUNKS + phase * TILES + 1))
                nc.scalar.activation(tile_of(sign[mat[phase + 1]], u), stage[:, s, :], ACT.Sign)\
                  .then_inc(sign_done, 1)

            def high(phase, u, s, first=False):
                step = u + phase * TILES
                act.wait_ge(full_ready, step + 1)
                if not first:
                    act.wait_ge(sums_done, 2 * step + GROUPS - 2)
                nc.scalar.copy(w_high[:, s, :], tile_of(base[mat[phase]], u)).then_inc(high_ready, 1)

            def silu(u, s):
                for half in range(2):
                    act.wait_ge(sums_done, u * 2 + (GROUPS + half + 1))
                    nc.scalar.activation(hidden_of(u, half), bank[2 * s + half][:], ACT.Silu)\
                      .then_inc(drained, 1)

            def hidden_high(u, first=False):
                for half in range(2):
                    if first:
                        act.wait_ge(drained, GROUPS + 2 * TILES + half + 1)
                    else:
                        act.wait_ge(sums_done, u * 2 + (GROUPS + 4 * TILES - 1 + half))
                    nc.scalar.copy(h_high[:, half, :], hidden_of(u, half)).then_inc(h_high_ready, 1)

            for b in range(PER_GROUP):
                act.dma_start(choices[b * C:(b + 1) * C, :, :], cond_w).then_inc(choices_in, 16)
            for c, groups in enumerate([[], [], [0, 1], [2, 3], [4, 5], [6, 7], []]):
                sign_w1(c)
                for g in groups:
                    y_group(g)
            high(gate, 0, 0, first=True)
            with act.Fori(0, PAIRS) as j:
                for s in range(2):
                    u = j * 2 + s
                    high(gate, u + 1, 1 - s)
                    signs(gate, u, s)
                    silu(u, s)
            high(gate, TILES - 1, 1)
            signs(gate, TILES - 2, 0)
            signs(gate, TILES - 1, 1)
            silu(TILES - 2, 0)
            high(up, 0, 0)
            silu(TILES - 1, 1)
            with act.Fori(0, PAIRS) as j:
                for s in range(2):
                    u = j * 2 + s
                    high(up, u + 1, 1 - s)
                    signs(up, u, s)
            high(up, TILES - 1, 1)
            signs(up, TILES - 2, 0)
            signs(up, TILES - 1, 1)
            high(down, 0, 0)
            hidden_high(0, first=True)
            act.wait_ge(drained, GROUPS + 4 * TILES)
            with act.Fori(0, PAIRS) as j:
                for s in range(2):
                    u = j * 2 + s
                    high(down, u + 1, 1 - s)
                    hidden_high(u + 1)
            high(down, TILES - 1, 1)
            hidden_high(TILES - 1)

        @block.vector
        def _(dve):
            def y_group(g):
                dve.wait_ge(y_high_ready, g + 1)
                src = bank[Y_BANKS[g % len(Y_BANKS)]][:].rearrange("p (k n) -> p k n", k=KT)
                t = slice(g * P, (g + 1) * P)
                nc.vector.tensor_tensor(y_low[:, :, t], src, y_high[:, :, t].bitcast(F32),
                                        ALU.subtract).then_inc(drained, 1)

            def absorb_w1(c):
                s = slice(c * CHUNK, (c + 1) * CHUNK)
                dve.wait_ge(w1_in[c], 32)
                nc.vector.tensor_tensor(w1_diff[:, s], w1_diff[:, s], base[0][:, s], ALU.subtract)\
                  .then_inc(diff_ready, 1)
                dve.wait_ge(diff_ready, c + 1)
                nc.vector.tensor_reduce(abs_sum[:, gate, c:c + 1], w1_diff[:, s], AX_X, ALU.add,
                                        apply_absolute_value=True).then_inc(abs_done, 1)

            def absorb(phase, u, pair, s):
                dve.wait_ge(stream_in[s], pair * 32 + (phase * TILES // 2 + 1) * 32)
                nc.vector.tensor_tensor(stage[:, s, :], stage[:, s, :],
                                        tile_of(base[mat[phase + 1]], u), ALU.subtract)\
                  .then_inc(diff_ready, 1)
                dve.wait_ge(diff_ready, u + (CHUNKS + phase * TILES + 1))
                nc.vector.tensor_reduce(abs_sum[:, phase + 1, bass.ds(u, 1)], stage[:, s, :], AX_X,
                                        ALU.add, apply_absolute_value=True).then_inc(abs_done, 1)

            def coefficient(phase, parts):
                dve.wait_ge(mean_summed, phase + 1)
                nc.vector.tensor_reduce(coeff[:, phase:phase + 1], bank[MEAN_BANK][:, 0:parts], AX_X,
                                        ALU.add).then_inc(coeff_ready, 1)
                dve.wait_ge(coeff_ready, phase + 1)
                dve.wait_ge(sign_done, CHUNKS + phase * TILES)

            def full(phase, u):
                b = tile_of(base[mat[phase]], u)
                nc.vector.scalar_tensor_tensor(out=b, in0=tile_of(sign[mat[phase]], u),
                                               scalar=coeff[:, phase:phase + 1], in1=b,
                                               op0=ALU.mult, op1=ALU.add).then_inc(full_ready, 1)

            def low(phase, u, s):
                dve.wait_ge(high_ready, u + (phase * TILES + 1))
                nc.vector.tensor_tensor(w_low[:, s, :], tile_of(base[mat[phase]], u),
                                        w_high[:, s, :].bitcast(F32), ALU.subtract)\
                  .then_inc(low_ready, 1)

            def times_up(u, s):
                for half in range(2):
                    dve.wait_ge(sums_done, u * 2 + (GROUPS + 2 * TILES + half + 1))
                    h = hidden_of(u, half)
                    nc.vector.tensor_tensor(h, bank[2 * s + half][:], h, ALU.mult).then_inc(drained, 1)

            def hidden_low(u):
                for half in range(2):
                    dve.wait_ge(h_high_ready, u * 2 + half + 1)
                    nc.vector.tensor_tensor(h_low[:, half, :], hidden_of(u, half),
                                            h_high[:, half, :].bitcast(F32), ALU.subtract)\
                      .then_inc(h_low_ready, 1)

            def pick_mix():
                dve.wait_ge(number_ready, 1)
                dve.wait_ge(itok_in, 16 * PER_GROUP)
                nc.vector.tensor_tensor(
                    chosen, number, itok[:].unsqueeze(1).to_broadcast([P, CANDIDATES, GROUPS]),
                    ALU.is_equal).then_inc(chosen_ready, 1)
                dve.wait_ge(chosen_ready, 1)
                dve.wait_ge(choices_in, 16 * PER_GROUP)
                for n in range(CANDIDATES):
                    if n:
                        dve.wait_ge(mix_chosen, n)
                    nc.vector.copy_predicated(
                        mix, chosen[:, n, :].unsqueeze(2).to_broadcast([P, GROUPS, C]),
                        choices[:, n, :].unsqueeze(1).to_broadcast([P, GROUPS, C])).then_inc(mix_chosen, 1)
                dve.wait_ge(mix_chosen, CANDIDATES)
                dve.wait_ge(diag_zeroed, 1)
                for b in range(PER_GROUP):
                    s = slice(b * C, (b + 1) * C)
                    nc.vector.tensor_copy(mix_diag[s, :, s], mix[s, :, :]).then_inc(mix_ready, 1)

            nc.vector.memset(mean_of[:], 1.0 / COUNT).then_inc(const_ready, 1)
            nc.vector.memset(mix, 0.0).then_inc(const_ready, 1)
            dve.wait_ge(const_ready, 2)
            pick_mix()
            for c, groups in enumerate([[], [], [0, 1], [2, 3], [4, 5], [6, 7], []]):
                absorb_w1(c)
                for g in groups:
                    y_group(g)
            coefficient(gate, CHUNKS)
            full(gate, 0)
            full(gate, 1)
            low(gate, 0, 0)
            for phase in (gate, up):
                if phase == up:
                    dve.wait_ge(drained, GROUPS + 2 * TILES)
                with dve.Fori(0, PAIRS) as j:
                    for s in range(2):
                        u = j * 2 + s
                        full(phase, u + 2)
                        low(phase, u + 1, 1 - s)
                        absorb(phase, u, j, s)
                        if phase == up:
                            times_up(u, s)
                low(phase, TILES - 1, 1)
                absorb(phase, TILES - 2, TILES // 2 - 1, 0)
                absorb(phase, TILES - 1, TILES // 2 - 1, 1)
                if phase == up:
                    times_up(TILES - 2, 0)
                coefficient(phase + 1, TILES)
                full(phase + 1, 0)
                full(phase + 1, 1)
                low(phase + 1, 0, 0)
                if phase == up:
                    times_up(TILES - 1, 1)
            hidden_low(0)
            with dve.Fori(0, PAIRS) as j:
                for s in range(2):
                    u = j * 2 + s
                    full(down, u + 2)
                    low(down, u + 1, 1 - s)
                    hidden_low(u + 1)
            low(down, TILES - 1, 1)
            hidden_low(TILES - 1)
            dve.wait_ge(residual_in, 16)
            for g in range(GROUPS):
                dve.wait_ge(group_done, g + 1)
                nc.vector.tensor_tensor(result[:, g, :], bank[(g + 4) % 8][:], result[:, g, :],
                                        ALU.add).then_inc(result_ready, 1)


def kernel(**inputs):
    import numpy as np
    import concourse.bacc as bacc
    from concourse.bass_utils import run_bass_kernel_spmd

    def inner_columns(a):
        n, h = a.shape
        return np.ascontiguousarray(
            a.reshape(n // P, P, h // P, P).transpose(3, 0, 2, 1).reshape(P, n // P, h))

    def inner_rows(a):
        h, n = a.shape
        return np.ascontiguousarray(a.reshape(h, n // P, P).transpose(2, 1, 0))

    a = {k: np.asarray(v) for k, v in inputs.items()}
    x = np.ascontiguousarray(a["x"])
    c = x.shape[1]
    per_group = P // c
    cond = a["itok_B_0_15"]
    arrays = {
        "x": x,
        "cond": np.ascontiguousarray(cond.reshape(-1, per_group).T),
        "cond_w": np.ascontiguousarray(a["L0_cond_weights"].transpose(1, 0, 2)),
        "w1": inner_columns(a["L0_ffn_w1"]),
        "m1": inner_columns(a["L0_ffn_mean_w1"]),
        "w3": inner_columns(a["L0_ffn_w3"]),
        "m3": inner_columns(a["L0_ffn_mean_w3"]),
        "w2": inner_rows(a["L0_ffn_w2"]),
        "m2": inner_rows(a["L0_ffn_mean_w2"]),
    }
    nc = bacc.Bacc("TRN2", target_bir_lowering=False, num_devices=1)
    args = [nc.dram_tensor(f"in_{k}", v.shape, mybir.dt.from_np(v.dtype), kind="ExternalInput").ap()
            for k, v in arrays.items()]
    args.append(nc.dram_tensor("out", x.shape, F32, kind="ExternalOutput").ap())
    adaln_ffn(nc, *args)
    r = run_bass_kernel_spmd(nc, [{f"in_{k}": v for k, v in arrays.items()}], core_ids=[0])
    return r.results[0]["out"]
```

```python
from contextlib import ExitStack

import concourse.bass as bass
from concourse import mybir

P = 128
F32 = mybir.dt.float32
F32R = mybir.dt.float32r
BF16 = mybir.dt.bfloat16
I32 = mybir.dt.int32
ALU = mybir.AluOpType
ACT = mybir.ActivationFunctionType
AX_X = mybir.AxisListType.X


def adaln_ffn(nc, x, cond, cond_w, w1, m1, w3, m3, w2, m2, out):
    HIDDEN = x.shape[2]
    TOKENS = x.shape[0] * x.shape[1]
    C = x.shape[1]
    TILES = w1.shape[1]
    UNIT = w1.shape[2]
    KT = HIDDEN // P
    GROUPS = TOKENS // P
    CANDIDATES = cond_w.shape[1]
    BITS = CANDIDATES.bit_length() - 1
    PER_GROUP = P // C
    HALF = TOKENS // 2
    HG = GROUPS // 2
    COUNT = TILES * UNIT * P
    W1_CHUNKS = [(u * UNIT, 2 * UNIT) for u in range(0, TILES - 2, 2)] + [
        ((TILES - 2) * UNIT, UNIT),
        ((TILES - 1) * UNIT, UNIT // 2), ((TILES - 1) * UNIT + UNIT // 2, UNIT // 2)]
    CHUNKS = len(W1_CHUNKS)
    PAIRS = TILES // 2 - 1
    WARM_UP = 14
    EARLY = 2
    assert UNIT == HIDDEN == HALF == 512 and TILES % 2 == 0 and PER_GROUP * C == P
    assert CANDIDATES == 1 << BITS

    with ExitStack() as ctx:
        def sb(name, shape, dt):
            return ctx.enter_context(nc.sbuf_tensor(name, shape, dt))

        def sem(name):
            return ctx.enter_context(nc.semaphore(name))

        y_high = sb("y_high", [P, KT, TOKENS], F32R)
        y_low = sb("y_low", [P, KT, TOKENS], F32R)
        hidden = sb("hidden", [P, TILES * TOKENS], F32)
        base = [sb(f"base{i}", [P, TILES * UNIT], F32) for i in range(2)]
        sign = [sb(f"sign{i}", [P, TILES * UNIT], BF16) for i in range(2)]
        stage = sb("stage", [P, 2, UNIT], F32)
        w_high = sb("w_high", [P, 2, UNIT], F32R)
        w_low = sb("w_low", [P, 2, UNIT], F32R)
        h_high = sb("h_high", [P, 4, HALF], F32R)
        h_low = sb("h_low", [P, 4, HALF], F32R)
        mean_of = sb("mean_of", [P, P], F32)
        abs_sum = sb("abs_sum", [P, 3, TILES], F32)
        coeff = sb("coeff", [P, 3], F32)
        warm = sb("warm", [P, 1], F32)
        itok = sb("itok", [P, GROUPS], I32)
        bit = sb("bit", [P, BITS, GROUPS], I32)
        rest = sb("rest", [P, BITS, GROUPS], I32)

        at = 0
        x_in = hidden[:, at:at + GROUPS * HIDDEN].rearrange("p (g t) -> p g t", g=GROUPS)
        at += GROUPS * HIDDEN
        mix_diag = hidden[:, at:at + GROUPS * P].rearrange("p (g n) -> p g n", g=GROUPS)
        at += GROUPS * P
        assert at <= TILES * (TOKENS - UNIT)
        w1_diff = hidden[:, TILES * (TOKENS - UNIT):]
        choices = base[1][:, 0:CANDIDATES * C].rearrange("p (s d) -> p s d", s=CANDIDATES)
        LEFT = CANDIDATES // 2 * HG * C
        left = [base[1][:, CANDIDATES * C + half * LEFT:][:, 0:LEFT]
                .rearrange("p (s g d) -> p s g d", s=CANDIDATES // 2, g=HG) for half in range(2)]
        result = base[1][:, 0:GROUPS * HIDDEN].rearrange("p (g t) -> p g t", g=GROUPS)

        bank = [ctx.enter_context(nc.psum_tensor(f"bank{i}", [P, 512], F32)) for i in range(8)]
        MEAN_BANK = 7
        STEP_BANKS = [[4, 5], [2, 3]]
        BASE_BANKS = [[0, 1], [4, 5]]
        SIGN_BANKS = [[2, 3], [0, 1]]
        OUT_BANKS = [0, 1, 6, 7, 4, 5, 2, 3]

        itok_in = sem("itok_in")
        choices_in = sem("choices_in")
        diag_zeroed = sem("diag_zeroed")
        x_loaded = [sem(f"x_loaded{i}") for i in range(2)]
        w1_in = [sem(f"w1_in{c}") for c in range(CHUNKS)]
        stream_in = [sem(f"stream_in{i}") for i in range(2)]
        residual_in = sem("residual_in")
        out_done = sem("out_done")
        early_sign_ready = sem("early_sign_ready")
        early_base_summed = sem("early_base_summed")
        early_base_read = sem("early_base_read")
        early_gate_ready = sem("early_gate_ready")
        bits_ready = sem("bits_ready")
        left_copied = sem("left_copied")
        mix_chosen = sem("mix_chosen")
        mix_ready = sem("mix_ready")
        const_ready = sem("const_ready")
        y_high_ready = sem("y_high_ready")
        diff_ready = sem("diff_ready")
        sign_done = sem("sign_done")
        abs_done = sem("abs_done")
        w1_sign_done = sem("w1_sign_done")
        act_abs_done = sem("act_abs_done")
        mean_summed = sem("mean_summed")
        coeff_ready = sem("coeff_ready")
        full_ready = sem("full_ready")
        high_ready = sem("high_ready")
        front_full_ready = sem("front_full_ready")
        front_high_ready = sem("front_high_ready")
        front_low_ready = sem("front_low_ready")
        low_ready = sem("low_ready")
        sums_done = sem("sums_done")
        drained = sem("drained")
        h_high_ready = sem("h_high_ready")
        h_low_ready = sem("h_low_ready")
        group_done = sem("group_done")
        result_ready = sem("result_ready")

        gate, up, down = 0, 1, 2
        mat = {gate: 0, up: 1, down: 0}

        def chunk(c):
            first, columns = W1_CHUNKS[c]
            return slice(first, first + columns)

        def tile_of(buf, u):
            return buf[:, bass.ds(u * UNIT, UNIT)]

        def hidden_of(u, half):
            return hidden[:, bass.ds(u * TOKENS + half * HALF, HALF)]

        FRONT, BACK = slice(0, UNIT // 2), slice(UNIT // 2, UNIT)
        AHEAD = 2
        ACT_SUMS = CHUNKS - AHEAD

        block = ctx.enter_context(nc.Block())

        @block.sync
        def _(sp):
            sp.dma_start(itok[:], cond).then_inc(itok_in, 16)
            sp.dma_start(choices, cond_w).then_inc(choices_in, 16)
            x_dram = x.rearrange("(g b) c t -> (b c) g t", g=GROUPS)
            for i in range(2):
                g = slice(i * HG, (i + 1) * HG)
                sp.dma_start(x_in[:, g, :], x_dram[:, g, :]).then_inc(x_loaded[i], 16)
            w1_flat = w1.rearrange("p u n -> p (u n)")
            m1_flat = m1.rearrange("p u n -> p (u n)")
            for c in range(CHUNKS):
                s = chunk(c)
                sp.dma_start(base[0][:, s], m1_flat[:, s]).then_inc(w1_in[c], 16)
                sp.dma_start(w1_diff[:, s], w1_flat[:, s]).then_inc(w1_in[c], 16)

            def stream(phase, w, m):
                with sp.Fori(0, TILES // 2) as j:
                    for s in range(2):
                        u = j * 2 + s
                        v = phase * TILES + u
                        sp.wait_ge(sign_done, v - 1 + AHEAD)
                        sp.wait_ge(abs_done, v - 1 + AHEAD)
                        sp.dma_start(stage[:, s, :], w[:, bass.ds(u, 1), :]).then_inc(stream_in[s], 16)
                        sp.dma_start(tile_of(base[mat[phase + 1]], u), m[:, bass.ds(u, 1), :])\
                          .then_inc(stream_in[s], 16)

            stream(gate, w3, m3)
            sp.wait_ge(low_ready, TILES)
            stream(up, w2, m2)
            sp.wait_ge(low_ready, 2 * TILES)
            sp.dma_start(result, x_dram).then_inc(residual_in, 16)
            out_dram = out.rearrange("(g b) c t -> (b c) g t", g=GROUPS)
            for g in range(GROUPS):
                sp.wait_ge(result_ready, g + 1)
                sp.dma_start(out_dram[:, g, :], result[:, g, :]).then_inc(out_done, 16)
            sp.wait_ge(out_done, 16 * GROUPS)

        @block.gpsimd
        def _(pool):
            nc.gpsimd.memset(mix_diag, 0.0).then_inc(diag_zeroed, 1)

        @block.tensor
        def _(pe):
            pe.wait_ge(const_ready, 1)
            for _ in range(WARM_UP):
                nc.tensor.matmul(bank[MEAN_BANK][:, 0:P], mean_of[:], mean_of[:], start=True, stop=True)

            for g in range(GROUPS):
                pe.wait_ge(mix_ready, (g // HG + 1) * PER_GROUP)
                pe.wait_ge(x_loaded[g // HG], 16)
                for k in range(KT):
                    last = nc.tensor.matmul(bank[g][:, k * P:(k + 1) * P],
                                            x_in[:, g, k * P:(k + 1) * P], mix_diag[:, g, :],
                                            start=True, stop=True)
                last.then_inc(sums_done, 1)

            def mean(phase, parts):
                pe.wait_ge(abs_done, AHEAD + phase * TILES)
                if phase == gate:
                    pe.wait_ge(act_abs_done, ACT_SUMS)
                nc.tensor.matmul(bank[MEAN_BANK][:, 0:parts], mean_of[:], abs_sum[:, phase, 0:parts],
                                 start=True, stop=True).then_inc(mean_summed, 1)

            def project(phase, u, s, in_halves=False):
                step = u + phase * TILES
                if in_halves:
                    pe.wait_ge(front_low_ready, 1)
                else:
                    pe.wait_ge(low_ready, step + 1)
                for half in range(2):
                    pe.wait_ge(drained, 2 * step + GROUPS - 3 + half)
                    dst = bank[STEP_BANKS[s][half]][:]
                    t = slice(half * HALF, (half + 1) * HALF)
                    for k in range(KT):
                        if in_halves and half == 0 and k == KT // 2:
                            pe.wait_ge(low_ready, step + 1)
                        n = slice(k * P, (k + 1) * P)
                        nc.tensor.matmul(dst, w_high[:, s, n], y_high[:, k, t], start=(k == 0), stop=False)
                        nc.tensor.matmul(dst, w_high[:, s, n], y_low[:, k, t], start=False, stop=False)
                        last = nc.tensor.matmul(dst, w_low[:, s, n], y_high[:, k, t], start=False,
                                                stop=(k == KT - 1))
                    last.then_inc(sums_done, 1)

            def early_base(u):
                pe.wait_ge(low_ready, u + 1)
                for half in range(2):
                    pe.wait_ge(drained, (half + 1) * HG)
                    dst = bank[BASE_BANKS[u][half]][:]
                    t = slice(half * HALF, (half + 1) * HALF)
                    for k in range(KT):
                        n = slice(k * P, (k + 1) * P)
                        nc.tensor.matmul(dst, w_high[:, u, n], y_high[:, k, t], start=(k == 0), stop=False)
                        nc.tensor.matmul(dst, w_high[:, u, n], y_low[:, k, t], start=False, stop=False)
                        last = nc.tensor.matmul(dst, w_low[:, u, n], y_high[:, k, t], start=False,
                                                stop=(k == KT - 1))
                    last.then_inc(early_base_summed, 1)

            def early_sign(u):
                pe.wait_ge(early_sign_ready, u + 1)
                for half in range(2):
                    if u == 1:
                        pe.wait_ge(early_base_read, half + 1)
                        if half == 1:
                            mean(gate, CHUNKS)
                    dst = bank[SIGN_BANKS[u][half]][:]
                    t = slice(half * HALF, (half + 1) * HALF)
                    for k in range(KT):
                        n = slice(k * P, (k + 1) * P)
                        nc.tensor.matmul(dst, h_high[:, u, n], y_high[:, k, t], start=(k == 0), stop=False)
                        last = nc.tensor.matmul(dst, h_high[:, u, n], y_low[:, k, t], start=False,
                                                stop=(k == KT - 1))
                    last.then_inc(sums_done, 1)

            def add_tile(u_slot, g, start, stop):
                dst = bank[OUT_BANKS[g]][:]
                half, i = g // HG, g % HG
                n, h = slice(i * P, (i + 1) * P), 2 * u_slot + half
                nc.tensor.matmul(dst, h_high[:, h, n], w_high[:, u_slot, :], start=start, stop=False)
                nc.tensor.matmul(dst, h_high[:, h, n], w_low[:, u_slot, :], start=False, stop=False)
                return nc.tensor.matmul(dst, h_low[:, h, n], w_high[:, u_slot, :], start=False, stop=stop)

            def contract(u, s, first=False):
                pe.wait_ge(low_ready, u + 2 * TILES + 1)
                for half in range(2):
                    pe.wait_ge(h_low_ready, u * 2 + half + 1)
                    if first and half == 1:
                        pe.wait_ge(drained, GROUPS + 4 * TILES)
                    for i in range(HG):
                        last = add_tile(s, half * HG + i, first, False)
                    last.then_inc(sums_done, 1)

            def contract_last():
                pe.wait_ge(low_ready, 3 * TILES - 1)
                pe.wait_ge(h_low_ready, 2 * TILES - 3)
                for g in range(HG):
                    add_tile(0, g, False, False)
                pe.wait_ge(low_ready, 3 * TILES)
                pe.wait_ge(h_low_ready, 2 * TILES - 1)
                for g in range(HG):
                    add_tile(1, g, False, True).then_inc(group_done, 1)
                pe.wait_ge(h_low_ready, 2 * TILES)
                for g in range(HG, GROUPS):
                    add_tile(0, g, False, False)
                    add_tile(1, g, False, True).then_inc(group_done, 1)

            early_base(0)
            early_sign(0)
            early_base(1)
            early_sign(1)
            project(gate, EARLY, 0, in_halves=True)
            project(gate, EARLY + 1, 1)
            for phase in (gate, up):
                with pe.Fori(EARLY // 2 + 1 if phase == gate else 0, PAIRS) as j:
                    for s in range(2):
                        project(phase, j * 2 + s, s)
                project(phase, TILES - 2, 0)
                mean(phase + 1, TILES)
                project(phase, TILES - 1, 1)
            contract(0, 0, first=True)
            contract(1, 1)
            with pe.Fori(1, PAIRS) as j:
                for s in range(2):
                    contract(j * 2 + s, s)
            contract_last()

        @block.scalar
        def _(act):
            def y_group(g):
                act.wait_ge(sums_done, g + 1)
                src = bank[g][:].rearrange("p (k n) -> p k n", k=KT)
                nc.scalar.copy(y_high[:, :, g * P:(g + 1) * P], src).then_inc(y_high_ready, 1)

            def early_signs(u):
                act.wait_ge(diff_ready, 1)
                nc.scalar.activation(h_high[:, u, :], tile_of(w1_diff, u), ACT.Sign)\
                  .then_inc(early_sign_ready, 1)

            def signs_w1(u, done):
                nc.scalar.activation(tile_of(sign[0], u), tile_of(w1_diff, u), ACT.Sign).then_inc(done, 1)

            def signs(phase, u, s):
                act.wait_ge(diff_ready, u + (CHUNKS + phase * TILES + 1))
                nc.scalar.activation(tile_of(sign[mat[phase + 1]], u), stage[:, s, :], ACT.Sign)\
                  .then_inc(sign_done, 1)

            def abs_w1(c):
                s = chunk(c)
                act.wait_ge(diff_ready, c + 1)
                nc.scalar.activation(sign[0][:, s], w1_diff[:, s], ACT.Abs,
                                     accum_out=abs_sum[:, gate, c:c + 1]).then_inc(act_abs_done, 1)

            def early_high(u):
                act.wait_ge(w1_in[0], 32)
                nc.scalar.copy(w_high[:, u, :], tile_of(base[0], u)).then_inc(high_ready, 1)

            def early_read(u):
                for half in range(2):
                    act.wait_ge(early_base_summed, 2 * u + half + 1)
                    nc.scalar.copy(hidden_of(u, half), bank[BASE_BANKS[u][half]][:])\
                      .then_inc(drained if u else early_base_read, 1)

            def early_silu(u):
                for half in range(2):
                    act.wait_ge(early_gate_ready, 2 * u + half + 1)
                    last = nc.scalar.activation(hidden_of(u, half), hidden_of(u, half), ACT.Silu)
                    if u == 0:
                        last.then_inc(drained, 1)

            def high(phase, u, s):
                step = u + phase * TILES
                act.wait_ge(full_ready, step + 1 - EARLY)
                act.wait_ge(sums_done, 2 * step + GROUPS - 2)
                nc.scalar.copy(w_high[:, s, :], tile_of(base[mat[phase]], u)).then_inc(high_ready, 1)

            def silu(u, s):
                for half in range(2):
                    act.wait_ge(sums_done, u * 2 + (GROUPS + half + 1))
                    nc.scalar.activation(hidden_of(u, half), bank[STEP_BANKS[s][half]][:], ACT.Silu)\
                      .then_inc(drained, 1)

            def hidden_high(u, s, first=False):
                for half in range(2):
                    if first:
                        act.wait_ge(drained, GROUPS + 2 * TILES + half + 1)
                    else:
                        act.wait_ge(sums_done, u * 2 + (GROUPS + 4 * TILES - 3 + half))
                    nc.scalar.copy(h_high[:, 2 * s + half, :], hidden_of(u, half)).then_inc(h_high_ready, 1)

            act.wait_ge(const_ready, 1)
            nc.scalar.activation(warm[:], mean_of[:, 0:1], ACT.Silu)
            act.wait_ge(choices_in, 16)
            for half in range(2):
                n = CANDIDATES // 2
                nc.scalar.copy(left[half], choices[:, 0:n, :].unsqueeze(2).to_broadcast([P, n, HG, C]))\
                  .then_inc(left_copied, 1)
            for g in range(HG):
                y_group(g)
            early_high(0)
            for g in range(HG, GROUPS):
                y_group(g)
            early_high(1)
            early_signs(0)
            abs_w1(0)
            early_signs(1)
            abs_w1(1)
            act.wait_ge(act_abs_done, 2)
            signs_w1(EARLY, sign_done)
            signs_w1(EARLY + 1, sign_done)
            early_read(0)
            for c in range(2, ACT_SUMS):
                abs_w1(c)
            early_read(1)
            act.wait_ge(act_abs_done, ACT_SUMS)
            act.wait_ge(diff_ready, CHUNKS)
            act.wait_ge(sums_done, 2 * EARLY + GROUPS - 2)
            for columns, full_sem, high_sem in ((FRONT, front_full_ready, front_high_ready),
                                                (BACK, full_ready, high_ready)):
                act.wait_ge(full_sem, 1)
                nc.scalar.copy(w_high[:, 0, columns], tile_of(base[0], EARLY)[:, columns])\
                  .then_inc(high_sem, 1)
            early_silu(0)
            signs(gate, 0, 0)
            high(gate, EARLY + 1, 1)
            signs(gate, 1, 1)
            signs_w1(EARLY + 2, w1_sign_done)
            high(gate, EARLY + 2, 0)
            signs(gate, EARLY, 0)
            silu(EARLY, 0)
            signs_w1(EARLY + 3, w1_sign_done)
            signs(gate, EARLY + 1, 1)
            silu(EARLY + 1, 1)
            with act.Fori(EARLY // 2 + 1, PAIRS) as j:
                for s in range(2):
                    u = j * 2 + s
                    high(gate, u + 1, 1 - s)
                    signs_w1(u + 2, w1_sign_done)
                    signs(gate, u, s)
                    silu(u, s)
            high(gate, TILES - 1, 1)
            signs(gate, TILES - 2, 0)
            signs(gate, TILES - 1, 1)
            early_silu(1)
            silu(TILES - 2, 0)
            high(up, 0, 0)
            silu(TILES - 1, 1)
            with act.Fori(0, PAIRS) as j:
                for s in range(2):
                    u = j * 2 + s
                    high(up, u + 1, 1 - s)
                    signs(up, u, s)
            high(up, TILES - 1, 1)
            signs(up, TILES - 2, 0)
            signs(up, TILES - 1, 1)
            high(down, 0, 0)
            hidden_high(0, 0, first=True)
            act.wait_ge(drained, GROUPS + 4 * TILES)
            with act.Fori(0, PAIRS) as j:
                for s in range(2):
                    u = j * 2 + s
                    high(down, u + 1, 1 - s)
                    hidden_high(u + 1, 1 - s)
            high(down, TILES - 1, 1)
            hidden_high(TILES - 1, 1)

        @block.vector
        def _(dve):
            def y_group(g):
                dve.wait_ge(y_high_ready, g + 1)
                src = bank[g][:].rearrange("p (k n) -> p k n", k=KT)
                t = slice(g * P, (g + 1) * P)
                nc.vector.tensor_tensor(y_low[:, :, t], src, y_high[:, :, t].bitcast(F32),
                                        ALU.subtract).then_inc(drained, 1)

            def absorb_w1(c):
                s = chunk(c)
                dve.wait_ge(w1_in[c], 32)
                nc.vector.tensor_tensor(w1_diff[:, s], w1_diff[:, s], base[0][:, s], ALU.subtract)\
                  .then_inc(diff_ready, 1)
                if c >= ACT_SUMS:
                    dve.wait_ge(diff_ready, c + 1)
                    nc.vector.tensor_reduce(abs_sum[:, gate, c:c + 1], w1_diff[:, s], AX_X, ALU.add,
                                            apply_absolute_value=True).then_inc(abs_done, 1)

            def early_gate(u):
                for half in range(2):
                    dve.wait_ge(sums_done, GROUPS + 2 * u + half + 1)
                    if u == 0:
                        dve.wait_ge(early_base_read, half + 1)
                    else:
                        dve.wait_ge(drained, GROUPS + half + 1)
                    h = hidden_of(u, half)
                    nc.vector.scalar_tensor_tensor(out=h, in0=bank[SIGN_BANKS[u][half]][:],
                                                   scalar=coeff[:, gate:gate + 1], in1=h,
                                                   op0=ALU.mult, op1=ALU.add)\
                      .then_inc(early_gate_ready, 1)

            def absorb(phase, u, pair, s):
                dve.wait_ge(stream_in[s], pair * 32 + (phase * TILES // 2 + 1) * 32)
                nc.vector.tensor_tensor(stage[:, s, :], stage[:, s, :],
                                        tile_of(base[mat[phase + 1]], u), ALU.subtract)\
                  .then_inc(diff_ready, 1)
                dve.wait_ge(diff_ready, u + (CHUNKS + phase * TILES + 1))
                nc.vector.tensor_reduce(abs_sum[:, phase + 1, bass.ds(u, 1)], stage[:, s, :], AX_X,
                                        ALU.add, apply_absolute_value=True).then_inc(abs_done, 1)

            def coefficient(phase, parts):
                dve.wait_ge(mean_summed, phase + 1)
                nc.vector.tensor_reduce(coeff[:, phase:phase + 1], bank[MEAN_BANK][:, 0:parts], AX_X,
                                        ALU.add).then_inc(coeff_ready, 1)
                dve.wait_ge(coeff_ready, phase + 1)
                dve.wait_ge(sign_done, AHEAD + phase * TILES)

            def full(phase, u):
                b = tile_of(base[mat[phase]], u)
                nc.vector.scalar_tensor_tensor(out=b, in0=tile_of(sign[mat[phase]], u),
                                               scalar=coeff[:, phase:phase + 1], in1=b,
                                               op0=ALU.mult, op1=ALU.add).then_inc(full_ready, 1)

            def low(phase, u, s):
                dve.wait_ge(high_ready, u + (phase * TILES + 1))
                nc.vector.tensor_tensor(w_low[:, s, :], tile_of(base[mat[phase]], u),
                                        w_high[:, s, :].bitcast(F32), ALU.subtract)\
                  .then_inc(low_ready, 1)

            def times_up(u, s):
                for half in range(2):
                    dve.wait_ge(sums_done, u * 2 + (GROUPS + 2 * TILES + half + 1))
                    h = hidden_of(u, half)
                    nc.vector.tensor_tensor(h, bank[STEP_BANKS[s][half]][:], h, ALU.mult).then_inc(drained, 1)

            def hidden_low(u, s):
                for half in range(2):
                    dve.wait_ge(h_high_ready, u * 2 + half + 1)
                    nc.vector.tensor_tensor(h_low[:, 2 * s + half, :], hidden_of(u, half),
                                            h_high[:, 2 * s + half, :].bitcast(F32), ALU.subtract)\
                      .then_inc(h_low_ready, 1)

            def split_itok():
                dve.wait_ge(itok_in, 16)
                value = itok[:]
                for i in range(BITS):
                    weight = CANDIDATES >> (i + 1)
                    if i > 0:
                        dve.wait_ge(bits_ready, 2 * i)
                    nc.vector.tensor_scalar(bit[:, i, :], value, weight, None, ALU.is_ge)\
                      .then_inc(bits_ready, 1)
                    if i < BITS - 1:
                        dve.wait_ge(bits_ready, 2 * i + 1)
                        nc.vector.scalar_tensor_tensor(out=rest[:, i, :], in0=bit[:, i, :],
                                                       scalar=-float(weight), in1=value,
                                                       op0=ALU.mult, op1=ALU.add)\
                          .then_inc(bits_ready, 1)
                        value = rest[:, i, :]

            def pick_mix(half):
                groups = slice(half * HG, (half + 1) * HG)
                dve.wait_ge(left_copied, half + 1)
                for i in range(BITS):
                    n = CANDIDATES >> (i + 1)
                    if i == 0:
                        upper = choices[:, n:2 * n, :].unsqueeze(2).to_broadcast([P, n, HG, C])
                    else:
                        dve.wait_ge(mix_chosen, half * BITS + i)
                        upper = left[half][:, n:2 * n, :, :]
                    nc.vector.copy_predicated(
                        left[half][:, 0:n, :, :],
                        bit[:, i, groups].unsqueeze(1).unsqueeze(3).to_broadcast([P, n, HG, C]),
                        upper).then_inc(mix_chosen, 1)
                dve.wait_ge(mix_chosen, (half + 1) * BITS)
                for b in range(PER_GROUP):
                    s = slice(b * C, (b + 1) * C)
                    nc.vector.tensor_copy(mix_diag[s, groups, s], left[half][s, 0, :, :])\
                      .then_inc(mix_ready, 1)

            nc.vector.memset(mean_of[:], 1.0 / COUNT).then_inc(const_ready, 1)
            split_itok()
            dve.wait_ge(bits_ready, 2 * BITS - 1)
            dve.wait_ge(diag_zeroed, 1)
            for half in range(2):
                pick_mix(half)
            for g in range(HG):
                y_group(g)
            low(gate, 0, 0)
            for g in range(HG, GROUPS):
                y_group(g)
            for c in range(CHUNKS):
                absorb_w1(c)
                if c == 0:
                    low(gate, 1, 1)
            coefficient(gate, CHUNKS)
            w = tile_of(base[0], EARLY)
            for columns, full_sem in ((FRONT, front_full_ready), (BACK, full_ready)):
                nc.vector.scalar_tensor_tensor(out=w[:, columns], in0=tile_of(sign[0], EARLY)[:, columns],
                                               scalar=coeff[:, gate:gate + 1], in1=w[:, columns],
                                               op0=ALU.mult, op1=ALU.add).then_inc(full_sem, 1)
            dve.wait_ge(front_high_ready, 1)
            nc.vector.tensor_tensor(w_low[:, 0, FRONT], w[:, FRONT], w_high[:, 0, FRONT].bitcast(F32),
                                    ALU.subtract).then_inc(front_low_ready, 1)
            dve.wait_ge(high_ready, EARLY + 1)
            nc.vector.tensor_tensor(w_low[:, 0, BACK], w[:, BACK], w_high[:, 0, BACK].bitcast(F32),
                                    ALU.subtract).then_inc(low_ready, 1)
            full(gate, EARLY + 1)
            early_gate(0)
            absorb(gate, 0, 0, 0)
            low(gate, EARLY + 1, 1)
            absorb(gate, 1, 0, 1)
            dve.wait_ge(w1_sign_done, 1)
            full(gate, EARLY + 2)
            low(gate, EARLY + 2, 0)
            absorb(gate, EARLY, 1, 0)
            dve.wait_ge(w1_sign_done, 2)
            full(gate, EARLY + 3)
            absorb(gate, EARLY + 1, 1, 1)
            with dve.Fori(EARLY // 2 + 1, PAIRS) as j:
                for s in range(2):
                    u = j * 2 + s
                    low(gate, u + 1, 1 - s)
                    dve.wait_ge(w1_sign_done, u - 1)
                    full(gate, u + 2)
                    absorb(gate, u, j, s)
            low(gate, TILES - 1, 1)
            absorb(gate, TILES - 2, TILES // 2 - 1, 0)
            absorb(gate, TILES - 1, TILES // 2 - 1, 1)
            early_gate(1)
            coefficient(up, TILES)
            full(up, 0)
            full(up, 1)
            low(up, 0, 0)
            dve.wait_ge(drained, GROUPS + 2 * TILES)
            with dve.Fori(0, PAIRS) as j:
                for s in range(2):
                    u = j * 2 + s
                    full(up, u + 2)
                    low(up, u + 1, 1 - s)
                    absorb(up, u, j, s)
                    times_up(u, s)
            low(up, TILES - 1, 1)
            absorb(up, TILES - 2, TILES // 2 - 1, 0)
            absorb(up, TILES - 1, TILES // 2 - 1, 1)
            times_up(TILES - 2, 0)
            coefficient(down, TILES)
            full(down, 0)
            full(down, 1)
            low(down, 0, 0)
            hidden_low(0, 0)
            times_up(TILES - 1, 1)
            with dve.Fori(0, PAIRS) as j:
                for s in range(2):
                    u = j * 2 + s
                    full(down, u + 2)
                    low(down, u + 1, 1 - s)
                    hidden_low(u + 1, 1 - s)
            low(down, TILES - 1, 1)
            hidden_low(TILES - 1, 1)
            dve.wait_ge(residual_in, 16)
            for g in range(GROUPS):
                dve.wait_ge(group_done, g + 1)
                nc.vector.tensor_tensor(result[:, g, :], bank[OUT_BANKS[g]][:], result[:, g, :],
                                        ALU.add).then_inc(result_ready, 1)


def kernel(**inputs):
    import numpy as np
    import concourse.bacc as bacc
    from concourse.bass_utils import run_bass_kernel_spmd

    def inner_columns(a):
        n, h = a.shape
        return np.ascontiguousarray(
            a.reshape(n // P, P, h // P, P).transpose(3, 0, 2, 1).reshape(P, n // P, h))

    def inner_rows(a):
        h, n = a.shape
        return np.ascontiguousarray(a.reshape(h, n // P, P).transpose(2, 1, 0))

    a = {k: np.asarray(v) for k, v in inputs.items()}
    x = np.ascontiguousarray(a["x"])
    c = x.shape[1]
    per_group = P // c
    cond = a["itok_B_0_15"]
    arrays = {
        "x": x,
        "cond": np.ascontiguousarray(np.repeat(cond.reshape(-1, per_group).T, c, axis=0)),
        "cond_w": np.ascontiguousarray(np.tile(a["L0_cond_weights"].transpose(1, 0, 2), (per_group, 1, 1))),
        "w1": inner_columns(a["L0_ffn_w1"]),
        "m1": inner_columns(a["L0_ffn_mean_w1"]),
        "w3": inner_columns(a["L0_ffn_w3"]),
        "m3": inner_columns(a["L0_ffn_mean_w3"]),
        "w2": inner_rows(a["L0_ffn_w2"]),
        "m2": inner_rows(a["L0_ffn_mean_w2"]),
    }
    nc = bacc.Bacc("TRN2", target_bir_lowering=False, num_devices=1)
    args = [nc.dram_tensor(f"in_{k}", v.shape, mybir.dt.from_np(v.dtype), kind="ExternalInput").ap()
            for k, v in arrays.items()]
    args.append(nc.dram_tensor("out", x.shape, F32, kind="ExternalOutput").ap())
    adaln_ffn(nc, *args)
    r = run_bass_kernel_spmd(nc, [{f"in_{k}": v for k, v in arrays.items()}], core_ids=[0])
    return r.results[0]["out"]
```
